# Optimizing a Trainium2 kernel written in Bass

```python
import numpy as np
import jax
import jax.numpy as jnp

def _softmax(x, axis=-1):
    return jax.nn.softmax(x, axis=axis)

def _gelu(x):
    return jax.nn.gelu(x, approximate=True)

def _silu(x):
    return jax.nn.silu(x)

def _sigmoid(x):
    return jax.nn.sigmoid(x)

def _layernorm(x, axis=-1, eps=1e-05):
    m = jnp.mean(x, axis=axis, keepdims=True)
    v = jnp.var(x, axis=axis, keepdims=True)
    return (x - m) / jnp.sqrt(v + eps)

def _scatter_add(tgt, idx, src, axis=0):
    return tgt.at[idx].add(src)

def _segment_sum(src, seg, n):
    return jax.ops.segment_sum(src, seg, n)
kernel_name = 'mk_adj_resnorm_d1_adj_r2_46d33d'

def setup_inputs(seed: int=0):
    np.random.seed(seed)
    _w = jnp.asarray

    def _rec_inputs():
        import jax
        import jax.numpy as jnp
        _gk = jax.random.key(seed)
        x = -0.000929 + 1 * jax.random.normal(jax.random.fold_in(_gk, 1), (8192, 64), jnp.float32)
        _a = jax.random.bernoulli(jax.random.fold_in(_gk, 2), 0.000488281, (8192, 8192))
        _a = jnp.logical_or(_a, jnp.swapaxes(_a, -1, -2))
        _a = jnp.logical_or(_a, jnp.eye(8192, dtype=bool))
        _af = _a.astype(jnp.float32)
        _af = _af * jax.random.uniform(jax.random.fold_in(_gk, 3), (8192, 8192), jnp.float32, 0.05, 1)
        adj = _af
        return (x, adj)
    x, adj = _rec_inputs()

    def _L0_gnn_setup():
        import jax, jax.numpy as jnp
        import numpy as np
        P_DROP = 0.1
        key = jax.random.key(seed)
        k1, k2, k3 = jax.random.split(key, 3)
        N, D = (8192, 64)
        x = jax.random.normal(k1, (N, D), dtype=jnp.float32)
        adj = jax.random.uniform(k2, (N, N), dtype=jnp.float32)
        u = jax.random.uniform(k3, (N, D), dtype=jnp.float32)
        return {'x': x, 'adj': adj, 'u': u}
    _L0_gnn_all = _L0_gnn_setup()
    _L0_gnn_in = {k: v for k, v in _L0_gnn_all.items() if k in ('u',)}
    del _L0_gnn_all
    return {'x': x, 'adj': adj, 'L0_gnn_u': _L0_gnn_in['u']}

def reference(x, adj, L0_gnn_u):
    import jax
    import jax.numpy as jnp

    def _L0_gnn_ref(x, adj, u):
        import jax, jax.numpy as jnp
        import numpy as np
        P_DROP = 0.1
        keep = (u >= P_DROP).astype(x.dtype)
        x_drop = x * keep / (1.0 - P_DROP)
        return jnp.matmul(adj, x_drop)
    x = _layernorm(x + _L0_gnn_ref(x, adj, L0_gnn_u), axis=-1)
    return x

_drawn_inputs = setup_inputs


def setup_inputs(seed=0):
    import zlib

    import numpy as np

    out = dict(_drawn_inputs(seed))
    spreads = {}
    factors = {}
    for name, (base, spread) in spreads.items():
        noise = np.random.default_rng([zlib.crc32(name.encode()), seed]).standard_normal(out[name].shape)
        drawn = base * np.exp(spread * noise) if base else spread * noise
        out[name] = jnp.asarray(drawn.astype(out[name].dtype))
    for name, factor in factors.items():
        out[name] = (out[name] * factor).astype(out[name].dtype)
    return out
```

```python
import concourse.bass as bass
from concourse import mybir
from contextlib import ExitStack

N = 8192
D = 64
P = 128
KT = N // P
CG = 1024
HALF = CG // 2
G = N // CG
R = CG // P
TC = 2
NC = KT // TC
SLOTS = 16
PIECES = 4
PT = KT // PIECES
PIECE = PT * D
P_DROP = 0.1
EPS = 1e-5


def build(nc: bass.Bass, x: bass.AP, adj: bass.AP, u: bass.AP, out: bass.AP):
    fp32 = mybir.dt.float32
    ALU = mybir.AluOpType
    ACT = mybir.ActivationFunctionType

    x_rows = x.rearrange("(p t) d -> p (t d)", p=P)
    u_rows = u.rearrange("(p t) d -> p (t d)", p=P)
    out_rows = out.rearrange("(p t) d -> p (t d)", p=P)

    with ExitStack() as ctx:
        def sb(name, shape):
            return ctx.enter_context(nc.sbuf_tensor(name, shape, fp32))

        def sem(name):
            return ctx.enter_context(nc.semaphore(name))

        adj_ring = sb("adj_ring", [P, SLOTS, TC * CG])
        x_nat = sb("x_nat", [P, KT * D])
        u_nat = sb("u_nat", [P, KT * D])
        x_drop = sb("x_drop", [P, KT * D])
        identity = sb("identity", [P, P])
        acc_sb = sb("acc_sb", [P, HALF])
        summed = sb("summed", [P, R * D])
        stats = sb("stats", [P, R, 6])
        gap = sb("gap", [P, R])
        within = sb("within", [P, R])
        between = sb("between", [P, R])
        squares = sb("squares", [P, R])
        twice_mean = sb("twice_mean", [P, R])
        mean = sb("mean", [P, R])
        eps = sb("eps", [P, 1])
        std = sb("std", [P, R])
        rstd = sb("rstd", [P, R])
        normed = sb("normed", [P, R * D])

        acc = ctx.enter_context(nc.psum_tensor("acc", [P, HALF], fp32))
        back = [ctx.enter_context(nc.psum_tensor(f"back{b}", [P, HALF], fp32)) for b in range(2)]

        chunk_loaded = [sem(f"chunk_loaded{s}") for s in range(SLOTS)]
        chunk_used = sem("chunk_used")
        x_loaded = [sem(f"x_loaded{i}") for i in range(PIECES)]
        kept_ready = sem("kept_ready")
        drop_ready = sem("drop_ready")
        zeros_ready = sem("zeros_ready")
        identity_ready = sem("identity_ready")
        acc_copied = sem("acc_copied")
        back_ready = sem("back_ready")
        sum_ready = sem("sum_ready")
        stats_ready = sem("stats_ready")
        gap_ready = sem("gap_ready")
        parts_ready = sem("parts_ready")
        between_ready = sem("between_ready")
        squares_ready = sem("squares_ready")
        eps_ready = sem("eps_ready")
        std_ready = sem("std_ready")
        rstd_ready = sem("rstd_ready")
        normed_ready = sem("normed_ready")
        out_stored = sem("out_stored")

        block = ctx.enter_context(nc.Block())

        @block.sync
        def _(sp):
            for s in range(SLOTS):
                sp.dma_start(adj_ring[:, s, :], adj[s]).then_inc(chunk_loaded[s], 16)
            with sp.Fori(1, G * NC // SLOTS) as turn:
                for s in range(SLOTS):
                    sp.wait_ge(chunk_used, (turn - 1) * SLOTS + s + 1)
                    sp.dma_start(adj_ring[:, s, :], adj[turn * SLOTS + s]).then_inc(chunk_loaded[s], 16)

        @block.gpsimd
        def _(pool):
            nc.gpsimd.memset(eps[:], EPS).then_inc(eps_ready, 1)
            nc.gpsimd.memset(identity[:], 0.0).then_inc(zeros_ready, 1)
            pool.wait_ge(zeros_ready, 1)
            nc.gpsimd.affine_select(out=identity[:], in_=identity[:], compare_op=ALU.not_equal, fill=1.0,
                                    base=0, pattern=[[-1, P]], channel_multiplier=1).then_inc(identity_ready, 1)

        @block.scalar
        def _(act):
            for i in range(PIECES):
                cols = slice(i * PIECE, (i + 1) * PIECE)
                act.dma_start(x_nat[:, cols], x_rows[:, cols]).then_inc(x_loaded[i], 16)
                act.dma_start(u_nat[:, cols], u_rows[:, cols]).then_inc(x_loaded[i], 16)
            act.wait_ge(eps_ready, 1)
            with act.Fori(0, G) as g:
                act.wait_ge(chunk_used, (g + 1) * NC)
                for b in range(2):
                    cols = slice(b * HALF // 2, (b + 1) * HALF // 2)
                    nc.scalar.copy(acc_sb[:, cols], acc[:, cols]).then_inc(acc_copied, 1)
                act.wait_ge(squares_ready, g + 1)
                nc.scalar.activation(std[:], squares[:], ACT.Sqrt, scale=1.0 / D, bias=eps[:]).then_inc(std_ready, 1)
                act.wait_ge(normed_ready, g + 1)
                act.dma_start(out_rows[:, bass.ds(g * (R * D), R * D)], normed[:]).then_inc(out_stored, 16)
            act.wait_ge(out_stored, 16 * G)

        @block.tensor
        def _(pe):
            pe.wait_ge(identity_ready, 1)
            with pe.Fori(0, G) as g:
                for k in range(NC):
                    if k * TC % PT == 0:
                        pe.wait_ge(drop_ready, k * TC // PT + 1)
                    slot = k % SLOTS
                    pe.wait_ge(chunk_loaded[slot], (g * (NC // SLOTS) + k // SLOTS + 1) * 16)
                    for tt in range(TC):
                        t = k * TC + tt
                        w = x_drop[:, t * D:(t + 1) * D]
                        for h in range(2):
                            m = adj_ring[:, slot, tt * CG + h * HALF:tt * CG + (h + 1) * HALF]
                            last = nc.tensor.matmul(acc[h * D:(h + 1) * D, :], w, m,
                                                    start=(t == 0), stop=(t == KT - 1))
                    last.then_inc(chunk_used, 1)
                for b in range(2):
                    pe.wait_ge(acc_copied, g * 2 + b + 1)
                    for c in range(2):
                        last = nc.tensor.transpose(back[b][:, c * P:(c + 1) * P],
                                                   acc_sb[:, (b * 2 + c) * P:(b * 2 + c + 1) * P], identity[:])
                    last.then_inc(back_ready, 1)

        @block.vector
        def _(dve):
            for i in range(PIECES):
                cols = slice(i * PIECE, (i + 1) * PIECE)
                dve.wait_ge(x_loaded[i], 32)
                nc.vector.scalar_tensor_tensor(out=x_drop[:, cols], in0=u_nat[:, cols], scalar=P_DROP,
                                               in1=x_nat[:, cols], op0=ALU.is_ge, op1=ALU.mult
                                               ).then_inc(kept_ready, 1)
                dve.wait_ge(kept_ready, i + 1)
                nc.vector.tensor_scalar(x_drop[:, cols], x_drop[:, cols], 1.0 / (1.0 - P_DROP), None,
                                        ALU.mult).then_inc(drop_ready, 1)
            with dve.Fori(0, G) as g:
                width = R * D // 2
                for b in range(2):
                    dve.wait_ge(back_ready, g * 2 + b + 1)
                    cols = slice(b * width, (b + 1) * width)
                    nc.vector.tensor_tensor(summed[:, cols], back[b][:, 0:width],
                                            x_nat[:, bass.ds(g * (R * D) + b * width, width)],
                                            ALU.add).then_inc(sum_ready, 1)
                for r in range(R):
                    if r % (R // 2) == 0:
                        dve.wait_ge(sum_ready, g * 2 + r // (R // 2) + 1)
                    last = nc.vector.bn_stats(stats[:, r, :], summed[:, r * D:(r + 1) * D])
                last.then_inc(stats_ready, 1)
                m0, q0, m1, q1 = (stats[:, :, i] for i in (1, 2, 4, 5))
                dve.wait_ge(stats_ready, g + 1)
                nc.vector.tensor_tensor(gap[:], m0, m1, ALU.subtract).then_inc(gap_ready, 1)
                nc.vector.tensor_tensor(within[:], q0, q1, ALU.add)
                nc.vector.tensor_tensor(twice_mean[:], m0, m1, ALU.add).then_inc(parts_ready, 1)
                dve.wait_ge(gap_ready, g + 1)
                nc.vector.scalar_tensor_tensor(out=between[:], in0=gap[:], scalar=D / 4, in1=gap[:],
                                               op0=ALU.mult, op1=ALU.mult).then_inc(between_ready, 1)
                dve.wait_ge(parts_ready, g + 1)
                nc.vector.tensor_scalar(mean[:], twice_mean[:], 0.5, None, ALU.mult)
                dve.wait_ge(between_ready, g + 1)
                nc.vector.tensor_tensor(squares[:], within[:], between[:], ALU.add).then_inc(squares_ready, 1)
                dve.wait_ge(std_ready, g + 1)
                nc.vector.reciprocal(rstd[:], std[:]).then_inc(rstd_ready, 1)
                dve.wait_ge(rstd_ready, g + 1)
                for r in range(R):
                    last = nc.vector.tensor_scalar(normed[:, r * D:(r + 1) * D], summed[:, r * D:(r + 1) * D],
                                                   mean[:, r:r + 1], rstd[:, r:r + 1],
                                                   ALU.subtract, ALU.mult)
                last.then_inc(normed_ready, 1)
                dve.wait_ge(normed_ready, g + 1)
                dve.wait_ge(out_stored, (g + 1) * 16)


def kernel(x, adj, L0_gnn_u):
    import numpy as np
    import concourse.bacc as bacc
    from concourse.bass_utils import run_bass_kernel_spmd

    x, adj, u = np.asarray(x), np.asarray(adj), np.asarray(L0_gnn_u)
    chunks = adj.reshape(P, G, R // 2, 2, P, NC, TC).transpose(1, 5, 4, 6, 3, 2, 0)
    chunks = np.ascontiguousarray(chunks).reshape(G * NC, P, TC * CG)
    arrays = {"x": x, "adj_chunks": chunks, "u": u}

    nc = bacc.Bacc("TRN2", target_bir_lowering=False, num_devices=1)
    args = [nc.dram_tensor(name, a.shape, mybir.dt.from_np(a.dtype), kind="ExternalInput").ap()
            for name, a in arrays.items()]
    out = nc.dram_tensor("out", (N, D), mybir.dt.float32, kind="ExternalOutput").ap()
    build(nc, *args, out)
    r = run_bass_kernel_spmd(nc, [arrays], core_ids=[0])
    return r.results[0]["out"]
```

```python
import concourse.bass as bass
from concourse import mybir
from contextlib import ExitStack

N = 8192
D = 64
P = 128
KT = N // P
P_DROP = 0.1
EPS = 1e-5

R = 8
FULL = 7
SHORT = [4, 2, 2]
SLOT = 2048
SLOTS = 16
CHUNKS = KT * KT * P // SLOT
NC = KT * R * P // SLOT
LAST_PARTS = 4
PIECES = 4
PT = KT // PIECES
PIECE = PT * D
HALF = R * P // 2

assert FULL * R + sum(SHORT) == KT
SHORT_GROUPS = [(FULL * R + sum(SHORT[:n]), rows, FULL * NC + sum(SHORT[:n]) * NC // R)
                for n, rows in enumerate(SHORT)]


def build(nc: bass.Bass, x: bass.AP, adj: bass.AP, u: bass.AP, out: bass.AP):
    fp32 = mybir.dt.float32
    ALU = mybir.AluOpType
    ACT = mybir.ActivationFunctionType

    x_rows = x.rearrange("(p t) d -> p (t d)", p=P)
    u_rows = u.rearrange("(p t) d -> p (t d)", p=P)
    out_rows = out.rearrange("(p t) d -> p (t d)", p=P)

    with ExitStack() as ctx:
        def sb(name, shape):
            return ctx.enter_context(nc.sbuf_tensor(name, shape, fp32))

        def sem(name):
            return ctx.enter_context(nc.semaphore(name))

        adj_ring = sb("adj_ring", [P, SLOTS, SLOT])
        x_nat = sb("x_nat", [P, KT * D])
        u_nat = sb("u_nat", [P, KT * D])
        normed = u_nat
        x_drop = sb("x_drop", [P, KT * D])
        identity = sb("identity", [P, P])
        eps = sb("eps", [P, 1])
        acc_sb = sb("acc_sb", [P, HALF])
        summed = sb("summed", [P, R * D])
        stats = sb("stats", [P, R, 6])
        gap = sb("gap", [P, R])
        within = sb("within", [P, R])
        between = sb("between", [P, R])
        squares = sb("squares", [P, R])
        twice_mean = sb("twice_mean", [P, R])
        mean = sb("mean", [P, R])
        std = sb("std", [P, R])
        rstd = sb("rstd", [P, R])

        acc = ctx.enter_context(nc.psum_tensor("acc", [P, HALF], fp32))
        back = [ctx.enter_context(nc.psum_tensor(f"back{b}", [P, HALF], fp32)) for b in range(2)]

        chunk_loaded = [sem(f"chunk_loaded{s}") for s in range(SLOTS)]
        last_loaded = [sem(f"last_loaded{i}") for i in range(LAST_PARTS)]
        chunk_used = sem("chunk_used")
        x_loaded = [sem(f"x_loaded{i}") for i in range(PIECES)]
        kept_ready = sem("kept_ready")
        drop_ready = sem("drop_ready")
        zeros_ready = sem("zeros_ready")
        identity_ready = sem("identity_ready")
        acc_copied = sem("acc_copied")
        back_ready = sem("back_ready")
        sum_ready = sem("sum_ready")
        stats_ready = sem("stats_ready")
        gap_ready = sem("gap_ready")
        parts_ready = sem("parts_ready")
        between_ready = sem("between_ready")
        squares_ready = sem("squares_ready")
        eps_ready = sem("eps_ready")
        std_ready = sem("std_ready")
        rstd_ready = sem("rstd_ready")
        normed_ready = sem("normed_ready")
        out_stored = sem("out_stored")

        block = ctx.enter_context(nc.Block())

        @block.sync
        def _(sp):
            for s in range(SLOTS):
                sp.dma_start(adj_ring[:, s, :], adj[s]).then_inc(chunk_loaded[s], 16)
            with sp.Fori(1, CHUNKS // SLOTS - 1) as turn:
                for s in range(SLOTS):
                    sp.wait_ge(chunk_used, (turn - 1) * SLOTS + s + 1)
                    sp.dma_start(adj_ring[:, s, :], adj[turn * SLOTS + s]).then_inc(chunk_loaded[s], 16)
            first = CHUNKS - SLOTS
            for s in range(SLOTS - 1):
                sp.wait_ge(chunk_used, first - SLOTS + s + 1)
                sp.dma_start(adj_ring[:, s, :], adj[first + s]).then_inc(chunk_loaded[s], 16)
            sp.wait_ge(chunk_used, CHUNKS - SLOTS)
            for i in range(LAST_PARTS):
                cols = slice(i * SLOT // LAST_PARTS, (i + 1) * SLOT // LAST_PARTS)
                sp.dma_start(adj_ring[:, SLOTS - 1, cols], adj[CHUNKS - 1][:, cols]).then_inc(last_loaded[i], 16)

        @block.gpsimd
        def _(pool):
            nc.gpsimd.memset(eps[:], EPS).then_inc(eps_ready, 1)
            nc.gpsimd.memset(identity[:], 0.0).then_inc(zeros_ready, 1)
            pool.wait_ge(zeros_ready, 1)
            nc.gpsimd.affine_select(out=identity[:], in_=identity[:], compare_op=ALU.not_equal, fill=1.0,
                                    base=0, pattern=[[-1, P]], channel_multiplier=1).then_inc(identity_ready, 1)

        @block.scalar
        def _(act):
            def group(n, row, rows, chunks, parts):
                act.wait_ge(chunk_used, chunks)
                width = rows * P // 2 // parts
                for b in range(parts):
                    nc.scalar.copy(acc_sb[:, b * width:(b + 1) * width],
                                   acc[:, b * width:(b + 1) * width]).then_inc(acc_copied, 1)
                act.wait_ge(squares_ready, n + 1)
                nc.scalar.activation(std[:, 0:rows], squares[:, 0:rows], ACT.Sqrt, scale=1.0 / D,
                                     bias=eps[:]).then_inc(std_ready, 1)
                act.wait_ge(normed_ready, n + 1)
                act.dma_start(out_rows[:, bass.ds(row * D, rows * D)],
                              normed[:, bass.ds(row * D, rows * D)]).then_inc(out_stored, 16)

            for i in range(PIECES):
                cols = slice(i * PIECE, (i + 1) * PIECE)
                act.dma_start(x_nat[:, cols], x_rows[:, cols]).then_inc(x_loaded[i], 16)
                act.dma_start(u_nat[:, cols], u_rows[:, cols]).then_inc(x_loaded[i], 16)
            act.wait_ge(eps_ready, 1)
            with act.Fori(0, FULL) as g:
                group(g, g * R, R, (g + 1) * NC, 2)
            for n, (row, rows, chunk) in enumerate(SHORT_GROUPS):
                group(FULL + n, row, rows, chunk + rows * NC // R, 1)
            act.wait_ge(out_stored, 16 * (FULL + len(SHORT)))

        @block.tensor
        def _(pe):
            def product(rows, slot, tt, t):
                width = rows * P // 2
                for h in range(2):
                    at = tt * 2 * width + h * width
                    last = nc.tensor.matmul(acc[h * D:(h + 1) * D, 0:width], x_drop[:, t * D:(t + 1) * D],
                                            adj_ring[:, slot, at:at + width],
                                            start=(t == 0), stop=(t == KT - 1))
                return last

            def turn_back(rows, parts, done):
                for b in range(parts):
                    pe.wait_ge(acc_copied, done + b + 1)
                    for c in range(rows // 2 // parts):
                        at = (b * (rows // 2 // parts) + c) * P
                        last = nc.tensor.transpose(back[b][:, c * P:(c + 1) * P], acc_sb[:, at:at + P], identity[:])
                    last.then_inc(back_ready, 1)

            pe.wait_ge(identity_ready, 1)
            with pe.Fori(0, FULL) as g:
                tiles = SLOT // (R * P)
                for k in range(NC):
                    if k * tiles % PT == 0:
                        pe.wait_ge(drop_ready, k * tiles // PT + 1)
                    pe.wait_ge(chunk_loaded[k % SLOTS], (g * (NC // SLOTS) + k // SLOTS + 1) * 16)
                    for tt in range(tiles):
                        last = product(R, k % SLOTS, tt, k * tiles + tt)
                    last.then_inc(chunk_used, 1)
                turn_back(R, 2, g * 2)
            for n, (row, rows, chunk) in enumerate(SHORT_GROUPS):
                tiles = SLOT // (rows * P)
                for k in range(KT // tiles):
                    slot = (chunk + k) % SLOTS
                    final = chunk + k == CHUNKS - 1
                    if not final:
                        pe.wait_ge(chunk_loaded[slot], ((chunk + k) // SLOTS + 1) * 16)
                    for tt in range(tiles):
                        if final and tt * LAST_PARTS % tiles == 0:
                            pe.wait_ge(last_loaded[tt * LAST_PARTS // tiles], 16)
                        last = product(rows, slot, tt, k * tiles + tt)
                    last.then_inc(chunk_used, 1)
                turn_back(rows, 1, 2 * FULL + n)

        @block.vector
        def _(dve):
            def group(n, row, rows, parts, done):
                width = rows * D // parts
                for b in range(parts):
                    dve.wait_ge(back_ready, done + b + 1)
                    nc.vector.tensor_tensor(summed[:, b * width:(b + 1) * width], back[b][:, 0:width],
                                            x_nat[:, bass.ds(row * D + b * width, width)],
                                            ALU.add).then_inc(sum_ready, 1)
                for r in range(rows):
                    if r % (rows // parts) == 0:
                        dve.wait_ge(sum_ready, done + r * parts // rows + 1)
                    last = nc.vector.bn_stats(stats[:, r, :], summed[:, r * D:(r + 1) * D])
                last.then_inc(stats_ready, 1)
                m0, q0, m1, q1 = (stats[:, 0:rows, i] for i in (1, 2, 4, 5))
                dve.wait_ge(stats_ready, n + 1)
                nc.vector.tensor_tensor(gap[:, 0:rows], m0, m1, ALU.subtract).then_inc(gap_ready, 1)
                nc.vector.tensor_tensor(within[:, 0:rows], q0, q1, ALU.add)
                nc.vector.tensor_tensor(twice_mean[:, 0:rows], m0, m1, ALU.add).then_inc(parts_ready, 1)
                dve.wait_ge(gap_ready, n + 1)
                nc.vector.scalar_tensor_tensor(out=between[:, 0:rows], in0=gap[:, 0:rows], scalar=D / 4,
                                               in1=gap[:, 0:rows], op0=ALU.mult, op1=ALU.mult
                                               ).then_inc(between_ready, 1)
                dve.wait_ge(parts_ready, n + 1)
                nc.vector.tensor_scalar(mean[:, 0:rows], twice_mean[:, 0:rows], 0.5, None, ALU.mult)
                dve.wait_ge(between_ready, n + 1)
                nc.vector.tensor_tensor(squares[:, 0:rows], within[:, 0:rows], between[:, 0:rows],
                                        ALU.add).then_inc(squares_ready, 1)
                dve.wait_ge(std_ready, n + 1)
                nc.vector.reciprocal(rstd[:, 0:rows], std[:, 0:rows]).then_inc(rstd_ready, 1)
                dve.wait_ge(rstd_ready, n + 1)
                for r in range(rows):
                    last = nc.vector.tensor_scalar(normed[:, bass.ds((row + r) * D, D)], summed[:, r * D:(r + 1) * D],
                                                   mean[:, r:r + 1], rstd[:, r:r + 1],
                                                   ALU.subtract, ALU.mult)
                last.then_inc(normed_ready, 1)
                dve.wait_ge(normed_ready, n + 1)

            for i in range(PIECES):
                cols = slice(i * PIECE, (i + 1) * PIECE)
                dve.wait_ge(x_loaded[i], 32)
                nc.vector.scalar_tensor_tensor(out=x_drop[:, cols], in0=u_nat[:, cols], scalar=P_DROP,
                                               in1=x_nat[:, cols], op0=ALU.is_ge, op1=ALU.mult
                                               ).then_inc(kept_ready, 1)
                dve.wait_ge(kept_ready, i + 1)
                nc.vector.tensor_scalar(x_drop[:, cols], x_drop[:, cols], 1.0 / (1.0 - P_DROP), None,
                                        ALU.mult).then_inc(drop_ready, 1)
            with dve.Fori(0, FULL) as g:
                group(g, g * R, R, 2, g * 2)
            for n, (row, rows, _) in enumerate(SHORT_GROUPS):
                group(FULL + n, row, rows, 1, 2 * FULL + n)


def kernel(x, adj, L0_gnn_u):
    import numpy as np
    import concourse.bacc as bacc
    from concourse.bass_utils import run_bass_kernel_spmd

    x, adj, u = np.asarray(x), np.asarray(adj), np.asarray(L0_gnn_u)
    chunks = np.empty((CHUNKS, P, SLOT), adj.dtype)
    by_row = adj.reshape(P, KT, N)
    groups = [(g * R, R, g * NC) for g in range(FULL)] + SHORT_GROUPS
    for row, rows, first in groups:
        tiles = SLOT // (rows * P)
        n = KT // tiles
        part = by_row[:, row:row + rows].reshape(P, rows // 2, 2, P, n, tiles).transpose(4, 3, 5, 2, 1, 0)
        chunks[first:first + n].reshape(n, P, tiles, 2, rows // 2, P)[...] = part
    arrays = {"x": x, "adj_chunks": chunks, "u": u}

    nc = bacc.Bacc("TRN2", target_bir_lowering=False, num_devices=1)
    args = [nc.dram_tensor(name, a.shape, mybir.dt.from_np(a.dtype), kind="ExternalInput").ap()
            for name, a in arrays.items()]
    out = nc.dram_tensor("out", (N, D), mybir.dt.float32, kind="ExternalOutput").ap()
    build(nc, *args, out)
    r = run_bass_kernel_spmd(nc, [arrays], core_ids=[0])
    return r.results[0]["out"]
```
